# Optimizing a Trainium2 kernel written in Bass

```python
import numpy as np
import jax
import jax.numpy as jnp

def _softmax(x, axis=-1):
    return jax.nn.softmax(x, axis=axis)

def _gelu(x):
    return jax.nn.gelu(x, approximate=True)

def _silu(x):
    return jax.nn.silu(x)

def _sigmoid(x):
    return jax.nn.sigmoid(x)

def _layernorm(x, axis=-1, eps=1e-05):
    m = jnp.mean(x, axis=axis, keepdims=True)
    v = jnp.var(x, axis=axis, keepdims=True)
    return (x - m) / jnp.sqrt(v + eps)

def _scatter_add(tgt, idx, src, axis=0):
    return tgt.at[idx].add(src)

def _segment_sum(src, seg, n):
    return jax.ops.segment_sum(src, seg, n)
kernel_name = 'mk_cond_seq_d2_seqx_r2_78c132'

def setup_inputs(seed: int=0):
    np.random.seed(seed)
    _w = jnp.asarray

    def _rec_inputs():
        import jax
        import jax.numpy as jnp
        _rk = jax.random.key(seed)
        x = 7.22e-05 + 1 * jax.random.normal(jax.random.fold_in(_rk, 1), (4, 1024, 512), jnp.float32)
        _lenS = 1024 - jax.random.randint(jax.random.fold_in(_rk, 7), (4,), 0, max(1, 1024 // 4) + 1, jnp.int32)
        _lenS2 = 1024 - jax.random.randint(jax.random.fold_in(_rk, 8), (4,), 0, max(1, 1024 // 4) + 1, jnp.int32)
        cond_1024 = 0.0061147 + 1.02565 * jax.random.normal(jax.random.fold_in(_rk, 11), (4, 512), jnp.float32)
        return (x, cond_1024)
    x, cond_1024 = _rec_inputs()

    def _L0_cond_setup():
        import jax, jax.numpy as jnp
        import numpy as np
        DIM = 512
        FF_MULT = 2
        EPS = 1e-06

        def _ln(x):
            mu = jnp.mean(x, axis=-1, keepdims=True)
            var = jnp.mean(jnp.square(x - mu), axis=-1, keepdims=True)
            return (x - mu) * jax.lax.rsqrt(var + EPS)
        key = jax.random.key(seed)
        ks = jax.random.split(key, 12)
        b, n, d = (4, 1024, DIM)
        h = FF_MULT * d
        s = lambda fan_in: 1.0 / np.sqrt(fan_in)
        return {'x': jax.random.normal(ks[0], (b, n, d), jnp.float32), 't': jax.random.normal(ks[1], (b, d), jnp.float32), 'ada_w': jax.random.normal(ks[2], (d, 6 * d), jnp.float32) * s(d), 'ada_b': jnp.zeros((6 * d,), jnp.float32), 'ssm_w1': jax.random.normal(ks[3], (d, d), jnp.float32) * s(d), 'ssm_b1': jnp.zeros((d,), jnp.float32), 'ssm_w2': jax.random.normal(ks[4], (d, d), jnp.float32) * s(d), 'ssm_b2': jnp.zeros((d,), jnp.float32), 'ff_w1': jax.random.normal(ks[5], (d, h), jnp.float32) * s(d), 'ff_b1': jnp.zeros((h,), jnp.float32), 'ff_w2': jax.random.normal(ks[6], (h, d), jnp.float32) * s(h), 'ff_b2': jnp.zeros((d,), jnp.float32)}
    _L0_cond_all = _L0_cond_setup()
    _L0_cond_in = {k: v for k, v in _L0_cond_all.items() if k in ('ada_w', 'ada_b', 'ssm_w1', 'ssm_b1', 'ssm_w2', 'ssm_b2', 'ff_w1', 'ff_b1', 'ff_w2', 'ff_b2')}
    del _L0_cond_all

    def _L1_cond_setup():
        import jax, jax.numpy as jnp
        import numpy as np
        EPS = 1e-05

        def _sln(h, w, ln_g, ln_b, Wg, bg, Wb, bb):
            mu = jnp.mean(h, axis=-1, keepdims=True)
            var = jnp.mean((h - mu) ** 2, axis=-1, keepdims=True)
            ln = (h - mu) / jnp.sqrt(var + EPS) * ln_g + ln_b
            gamma = (w @ Wg.T + bg)[:, None, :]
            beta = (w @ Wb.T + bb)[:, None, :]
            return gamma * ln + beta
        key = jax.random.key(seed)
        ks = jax.random.split(key, 20)
        B, N, D = (4, 512, 512)
        F = 4 * D
        s = lambda fan: 1.0 / np.sqrt(fan)
        inp = {'hidden': jax.random.normal(ks[0], (B, N, D), jnp.float32), 'w': jax.random.normal(ks[1], (B, D), jnp.float32), 'ln_g': jnp.ones((D,), jnp.float32), 'ln_b': jnp.zeros((D,), jnp.float32), 'Wg': jax.random.normal(ks[2], (D, D), jnp.float32) * s(D), 'bg': jnp.zeros((D,), jnp.float32), 'Wb': jax.random.normal(ks[3], (D, D), jnp.float32) * s(D), 'bb': jnp.zeros((D,), jnp.float32), 'Wqkv': jax.random.normal(ks[4], (3 * D, D), jnp.float32) * s(D), 'bqkv': jnp.zeros((3 * D,), jnp.float32), 'Wp': jax.random.normal(ks[5], (D, D), jnp.float32) * s(D), 'bp': jnp.zeros((D,), jnp.float32), 'W1': jax.random.normal(ks[6], (F, D), jnp.float32) * s(D), 'b1': jnp.zeros((F,), jnp.float32), 'W2': jax.random.normal(ks[7], (D, F), jnp.float32) * s(F), 'b2': jnp.zeros((D,), jnp.float32), 'num_heads': 16}
        return inp
    _L1_cond_all = _L1_cond_setup()
    _L1_cond_in = {k: v for k, v in _L1_cond_all.items() if k in ('ln_g', 'ln_b', 'Wg', 'bg', 'Wb', 'bb', 'Wqkv', 'bqkv', 'Wp', 'bp', 'W1', 'b1', 'W2', 'b2')}
    del _L1_cond_all
    return {'x': x, 'cond_1024': cond_1024, 'L0_cond_ada_w': _L0_cond_in['ada_w'], 'L0_cond_ada_b': _L0_cond_in['ada_b'], 'L0_cond_ssm_w1': _L0_cond_in['ssm_w1'], 'L0_cond_ssm_b1': _L0_cond_in['ssm_b1'], 'L0_cond_ssm_w2': _L0_cond_in['ssm_w2'], 'L0_cond_ssm_b2': _L0_cond_in['ssm_b2'], 'L0_cond_ff_w1': _L0_cond_in['ff_w1'], 'L0_cond_ff_b1': _L0_cond_in['ff_b1'], 'L0_cond_ff_w2': _L0_cond_in['ff_w2'], 'L0_cond_ff_b2': _L0_cond_in['ff_b2'], 'L1_cond_ln_g': _L1_cond_in['ln_g'], 'L1_cond_ln_b': _L1_cond_in['ln_b'], 'L1_cond_Wg': _L1_cond_in['Wg'], 'L1_cond_bg': _L1_cond_in['bg'], 'L1_cond_Wb': _L1_cond_in['Wb'], 'L1_cond_bb': _L1_cond_in['bb'], 'L1_cond_Wqkv': _L1_cond_in['Wqkv'], 'L1_cond_bqkv': _L1_cond_in['bqkv'], 'L1_cond_Wp': _L1_cond_in['Wp'], 'L1_cond_bp': _L1_cond_in['bp'], 'L1_cond_W1': _L1_cond_in['W1'], 'L1_cond_b1': _L1_cond_in['b1'], 'L1_cond_W2': _L1_cond_in['W2'], 'L1_cond_b2': _L1_cond_in['b2']}

def reference(x, cond_1024, L0_cond_ada_w, L0_cond_ada_b, L0_cond_ssm_w1, L0_cond_ssm_b1, L0_cond_ssm_w2, L0_cond_ssm_b2, L0_cond_ff_w1, L0_cond_ff_b1, L0_cond_ff_w2, L0_cond_ff_b2, L1_cond_ln_g, L1_cond_ln_b, L1_cond_Wg, L1_cond_bg, L1_cond_Wb, L1_cond_bb, L1_cond_Wqkv, L1_cond_bqkv, L1_cond_Wp, L1_cond_bp, L1_cond_W1, L1_cond_b1, L1_cond_W2, L1_cond_b2):
    import jax
    import jax.numpy as jnp

    def _L0_cond_ref(x, t, ada_w, ada_b, ssm_w1, ssm_b1, ssm_w2, ssm_b2, ff_w1, ff_b1, ff_w2, ff_b2):
        import jax, jax.numpy as jnp
        import numpy as np
        DIM = 512
        FF_MULT = 2
        EPS = 1e-06

        def _ln(x):
            mu = jnp.mean(x, axis=-1, keepdims=True)
            var = jnp.mean(jnp.square(x - mu), axis=-1, keepdims=True)
            return (x - mu) * jax.lax.rsqrt(var + EPS)
        emb = jnp.dot(jax.nn.silu(t), ada_w) + ada_b
        shift_msa, scale_msa, gate_msa, shift_mlp, scale_mlp, gate_mlp = jnp.split(emb, 6, axis=-1)
        norm = _ln(x) * (1.0 + scale_msa[:, None]) + shift_msa[:, None]
        h = jax.nn.gelu(jnp.dot(norm, ssm_w1) + ssm_b1, approximate=False)
        ssm_out = jnp.dot(h, ssm_w2) + ssm_b2
        x = x + gate_msa[:, None] * ssm_out
        norm2 = _ln(x) * (1.0 + scale_mlp[:, None]) + shift_mlp[:, None]
        hf = jax.nn.gelu(jnp.dot(norm2, ff_w1) + ff_b1, approximate=True)
        ff_out = jnp.dot(hf, ff_w2) + ff_b2
        x = x + gate_mlp[:, None] * ff_out
        return x

    def _L1_cond_ref(hidden, w, ln_g, ln_b, Wg, bg, Wb, bb, Wqkv, bqkv, Wp, bp, W1, b1, W2, b2, num_heads):
        import jax, jax.numpy as jnp
        import numpy as np
        EPS = 1e-05

        def _sln(h, w, ln_g, ln_b, Wg, bg, Wb, bb):
            mu = jnp.mean(h, axis=-1, keepdims=True)
            var = jnp.mean((h - mu) ** 2, axis=-1, keepdims=True)
            ln = (h - mu) / jnp.sqrt(var + EPS) * ln_g + ln_b
            gamma = (w @ Wg.T + bg)[:, None, :]
            beta = (w @ Wb.T + bb)[:, None, :]
            return gamma * ln + beta
        B, N, D = hidden.shape
        hd = D // num_heads
        h = _sln(hidden, w, ln_g, ln_b, Wg, bg, Wb, bb)
        qkv = (h @ Wqkv.T + bqkv).reshape(B, N, num_heads, hd, 3)
        q = jnp.moveaxis(qkv[..., 0], 2, 1)
        k = jnp.moveaxis(qkv[..., 1], 2, 1)
        v = jnp.moveaxis(qkv[..., 2], 2, 1)
        energy = jnp.einsum('bhqd,bhkd->bhqk', q, k)
        att = jax.nn.softmax(energy, axis=-1) / D ** 0.5
        out = jnp.einsum('bhqk,bhkd->bhqd', att, v)
        out = jnp.moveaxis(out, 1, 2).reshape(B, N, D)
        out = out @ Wp.T + bp
        h1 = out + hidden
        h2 = _sln(h1, w, ln_g, ln_b, Wg, bg, Wb, bb)
        return h2 + h1
    x = _L0_cond_ref(x, cond_1024, L0_cond_ada_w, L0_cond_ada_b, L0_cond_ssm_w1, L0_cond_ssm_b1, L0_cond_ssm_w2, L0_cond_ssm_b2, L0_cond_ff_w1, L0_cond_ff_b1, L0_cond_ff_w2, L0_cond_ff_b2)
    x = _L1_cond_ref(x, cond_1024, L1_cond_ln_g, L1_cond_ln_b, L1_cond_Wg, L1_cond_bg, L1_cond_Wb, L1_cond_bb, L1_cond_Wqkv, L1_cond_bqkv, L1_cond_Wp, L1_cond_bp, L1_cond_W1, L1_cond_b1, L1_cond_W2, L1_cond_b2, 16)
    return x

_drawn_inputs = setup_inputs


def setup_inputs(seed=0):
    import zlib

    import numpy as np

    out = dict(_drawn_inputs(seed))
    spreads = {'L0_cond_ada_b': (0.0, 0.1),
     'L0_cond_ssm_b1': (0.0, 0.1),
     'L0_cond_ssm_b2': (0.0, 0.1),
     'L0_cond_ff_b1': (0.0, 0.1),
     'L0_cond_ff_b2': (0.0, 0.1),
     'L1_cond_ln_g': (1.0, 0.2),
     'L1_cond_ln_b': (0.0, 0.1),
     'L1_cond_bg': (0.0, 0.1),
     'L1_cond_bb': (0.0, 0.1),
     'L1_cond_bqkv': (0.0, 0.8),
     'L1_cond_bp': (0.0, 0.1),
     'L1_cond_b1': (0.0, 0.1),
     'L1_cond_b2': (0.0, 0.1)}
    factors = {}
    for name, (base, spread) in spreads.items():
        noise = np.random.default_rng([zlib.crc32(name.encode()), seed]).standard_normal(out[name].shape)
        drawn = base * np.exp(spread * noise) if base else spread * noise
        out[name] = jnp.asarray(drawn.astype(out[name].dtype))
    for name, factor in factors.items():
        out[name] = (out[name] * factor).astype(out[name].dtype)
    return out
```

```python
from contextlib import ExitStack

import concourse.bass as bass
from concourse import mybir

P = 128
B, N, D = 4, 1024, 512
T = B * N
FF = 2 * D
H, HD = 16, 32
KT = D // P
FT = FF // P
CH = 512
NCH = T // CH
TT = CH // P
G = B * KT
HG = P // HD
KC = N // P
QH = N // CH
RING = 3
STACK_LOADS = 9

L0_EPS, L1_EPS = 1e-6, 1e-5
F32 = mybir.dt.float32
F32R = mybir.dt.float32r
ALU = mybir.AluOpType
ACT = mybir.ActivationFunctionType
AX = mybir.AxisListType

SHIFT_MSA, SCALE_MSA, GATE_MSA, SHIFT_MLP, SCALE_MLP, GATE_MLP, GAMMA, BETA, SLN_S, SLN_T, BIAS_MSA, BIAS_MLP = range(12)
ROW_ORDER = (GAMMA, BETA, SHIFT_MSA, SCALE_MSA, SHIFT_MLP, SCALE_MLP, GATE_MSA, GATE_MLP)
TURNED = (SCALE_MSA, SHIFT_MSA, SCALE_MLP, SHIFT_MLP, SLN_S, SLN_T)
SPREAD = (GATE_MLP, GATE_MSA, SLN_S, SLN_T, BIAS_MLP, BIAS_MSA)
SPREAD_ORDER = (SLN_S, SLN_T, GATE_MSA, BIAS_MSA, GATE_MLP, BIAS_MLP)
C_B1, C_FB1, C_BQ, C_BK = 0, KT, KT + FT, KT + FT + KT
NCOL = KT + FT + 2 * KT
R_B2, R_FB2, R_BV, R_BP = range(4)

HI, LO = 0, 1
TERMS = ((HI, HI), (HI, LO), (LO, HI))


class Shared:
    pass


def add_bias(pe, sh, out):
    pe.matmul(out, sh.ones2[:], sh.bias_rows[:], start=True, stop=False)


def split_product(pe, out, stationary, moving, start, stop):
    for n, (a, b) in enumerate(TERMS):
        last = pe.matmul(out, stationary(a), moving(b), start=start and n == 0, stop=stop and n == len(TERMS) - 1)
    return last


def wait_apart(eng, passed, waits):
    for semaphore, value in waits:
        eng.wait_ge(semaphore, value)
    eng.sem_inc(passed, 1)


def early(nc, *specs):
    with ExitStack() as ctx:
        return [ctx.enter_context(nc.sbuf_tensor(*spec)) for spec in specs]


def load_stack(eng, sh, qs, ks, g, slot):
    for row, part in enumerate((HI, LO, HI)):
        src = sh.qk_d[1, part, g].rearrange("(j d) n -> d j n", d=HD)
        eng.dma_start(ks[HD * row:HD * (row + 1), slot].bitcast(F32), src).then_inc(sh.stack_loaded[slot], 16)
    for half in range(QH):
        for row, part in enumerate((HI, HI, LO)):
            src = sh.qk_d[0, part, g, :, half * CH:(half + 1) * CH].rearrange("(j d) n -> d j n", d=HD)
            eng.dma_start(qs[HD * row:HD * (row + 1), slot, half].bitcast(F32), src).then_inc(sh.stack_loaded[slot], 16)


def load_projection_input(eng, sh, a_f, x, st, b, half):
    for k in range(KT):
        eng.dma_start(a_f[:, half, k], sh.at_d[KT * b + k, :, half * CH:(half + 1) * CH]).then_inc(sh.a_loaded[half], 16)
    eng.dma_start(x[:, half], sh.x2_d[b * N + half * CH:b * N + (half + 1) * CH].rearrange("(t p) d -> p t d", p=P)).then_inc(sh.x_loaded[half], 16)
    for i in range(2):
        eng.dma_start(st[:, half, i], sh.rows_d[2 + i, b].partition_broadcast(P)).then_inc(sh.st_loaded[half], 16)


def split_in_place(eng, sh, n):
    return eng.tensor_tensor(sh.w0[:, LO, n, :], sh.w0_raw[:, LO, n, :], sh.w0[:, HI, n, :].bitcast(F32), ALU.subtract)


def raw_weight(sh, weights, n):
    return sh.w0_raw[:, LO, n, :].rearrange("p (k n) -> p k n", n=weights[n].shape[-1])


def setup_stage(nc, sh, x_in, cond_t, ada_w, wg_t, wb_t, row_bias, lngb, colpack, neg_mask, ident_in, weights):
    with ExitStack() as ctx:
        def sb(name, shape, dt=F32):
            return ctx.enter_context(nc.sbuf_tensor(name, shape, dt))

        def sem(name):
            return ctx.enter_context(nc.semaphore(name))

        SLOTS = 4
        mod_w = sb("mod_w", [P, SLOTS, KT, D])
        cond = sb("cond", [P, KT, B])
        silu = sb("silu", [P, KT, B])
        rows = sb("rows", [B, 12, D])
        lngb4 = sb("lngb4", [B, 2, D])
        br_raw = sb("br_raw", [2, D])
        br_hi = sb("br_hi", [2, D], F32R)
        mask2 = sb("su_mask2", [2, 1])
        stats = sb("su_stats", [P, TT, 6])
        mv = sb("su_mv", [P, TT, 2])
        ve = sb("su_ve", [P, TT])
        rstd = sb("su_rstd", [P, TT])

        cond_loaded = sem("su_cond_loaded")
        consts_loaded = sem("su_consts_loaded")
        x_loaded = sem("su_x_loaded")
        stats_ready, mv_ready = sem("su_stats_ready"), sem("su_mv_ready")
        ve_ready, rstd_ready = sem("su_ve_ready"), sem("su_rstd_ready")
        xn_ready = sem("su_xn_ready")
        mod_w_loaded = [sem(f"su_mod_w_loaded{i}") for i in range(SLOTS)]
        raw_loaded = [sem(f"su_raw_loaded{i}") for i in range(2)]
        silu_ready = sem("su_silu_ready")
        row_ps_ready = sem("su_row_ps_ready")
        rows_ready = sem("su_rows_ready")
        gb_step = sem("su_gb_step")
        bias_gated = sem("su_bias_gated")
        turned_ready = sem("su_turned_ready")
        mod_ready = sem("su_mod_ready")
        w_hi = sem("su_w_hi")
        w_lo = sem("su_w_lo")
        br_step = sem("su_br_step")
        rows_stored = sem("su_rows_stored")
        ps = sh.ps

        def raw_view(n):
            return raw_weight(sh, weights, n)

        block = ctx.enter_context(nc.Block())

        @block.sync
        def _(sp):
            for n in range(8):
                if n >= SLOTS:
                    sp.wait_ge(row_ps_ready, n - SLOTS + 1)
                row = ROW_ORDER[n]
                src = ada_w[:, row * D:(row + 1) * D] if row < 6 else (wg_t if row == GAMMA else wb_t)
                sp.dma_start(mod_w[:, n % SLOTS], src.rearrange("(k p) n -> p k n", p=P)).then_inc(mod_w_loaded[n % SLOTS], 16)
                if n in (4, 5):
                    sp.dma_start(raw_view(n - 4), weights[n - 4]).then_inc(raw_loaded[n - 4], 16)

        @block.scalar
        def _(act):
            act.dma_start(cond[:], cond_t).then_inc(cond_loaded, 16)
            act.dma_start(rows[:, 0:8, :], row_bias.partition_broadcast(B)).then_inc(consts_loaded, 16)
            act.dma_start(lngb4[:], lngb.partition_broadcast(B)).then_inc(consts_loaded, 16)
            act.dma_start(sh.cols[:], colpack).then_inc(consts_loaded, 16)
            act.dma_start(rows[:, BIAS_MSA:BIAS_MLP + 1, :], sh.biasrows_in[R_B2:R_FB2 + 1].partition_broadcast(B)).then_inc(consts_loaded, 16)
            act.dma_start(br_raw[:], sh.biasrows_in[R_BP].partition_broadcast(2)).then_inc(consts_loaded, 16)
            act.dma_start(mask2[:], neg_mask).then_inc(consts_loaded, 16)
            act.dma_start(sh.ident[:], ident_in).then_inc(consts_loaded, 16)
            act.dma_start(sh.xa[:], x_in[0:CH].rearrange("(t p) d -> p t d", p=P)).then_inc(x_loaded, 16)
            act.wait_ge(cond_loaded, 16)
            nc.scalar.activation(silu[:], cond[:], ACT.Silu).then_inc(silu_ready, 1)
            for n in range(2):
                act.wait_ge(raw_loaded[n], 16)
                nc.scalar.copy(sh.w0[:, HI, n, :], sh.w0_raw[:, LO, n, :]).then_inc(w_hi, 1)

        @block.tensor
        def _(pe):
            def turn_rows():
                pe.wait_ge(rows_ready, 6)
                pe.wait_ge(gb_step, 3)
                pe.wait_ge(consts_loaded, 7 * 16)
                for i, row in enumerate(TURNED):
                    for k in range(KT):
                        at = (i * KT + k) * B
                        last = pe.transpose(ps[0][:, at:at + B], rows[:, row, k * P:(k + 1) * P], sh.ident[0:B, 0:B])
                last.then_inc(turned_ready, 1)

            pe.wait_ge(cond_loaded, 16)
            for n, row in enumerate(ROW_ORDER):
                if n == 2:
                    pe.wait_ge(silu_ready, 1)
                if n == 7:
                    turn_rows()
                pe.wait_ge(mod_w_loaded[n % SLOTS], 16 * (n // SLOTS + 1))
                act_t = silu if row < 6 else cond
                for k in range(KT):
                    last = pe.matmul(ps[n][0:B, :], act_t[:, k, :], mod_w[:, n % SLOTS, k, :], start=k == 0, stop=k == KT - 1)
                last.then_inc(row_ps_ready, 1)

        @block.vector
        def _(dve):
            nc.vector.memset(sh.ones2[:].bitcast(F32), 1.0)
            dve.wait_ge(consts_loaded, 7 * 16)
            nc.vector.tensor_copy(br_hi[:], br_raw[:]).then_inc(br_step, 1)
            dve.wait_ge(br_step, 1)
            nc.vector.scalar_tensor_tensor(sh.bias_rows[:], br_hi[:].bitcast(F32), mask2[:, 0:1], br_raw[:], ALU.mult, ALU.add)
            dve.wait_ge(x_loaded, 16)
            for t in range(TT):
                nc.vector.bn_stats(stats[:, t, :], sh.xa[:, t, :]).then_inc(stats_ready, 1)
            for t in range(TT):
                dve.wait_ge(stats_ready, t + 1)
                nc.vector.bn_aggr(mv[:, t, :], stats[:, t, :]).then_inc(mv_ready, 1)
            dve.wait_ge(rstd_ready, 1)
            for t in range(TT):
                nc.vector.tensor_scalar(sh.xn1[:, t, :], sh.xa[:, t, :], mv[:, t, 0:1], rstd[:, t:t + 1],
                                        ALU.subtract, ALU.mult).then_inc(xn_ready, 1)
            for n, row in enumerate(ROW_ORDER):
                if n in (5, 7):
                    w = (n - 5) // 2
                    dve.wait_ge(w_hi, w + 1)
                    split_in_place(nc.vector, sh, w).then_inc(w_lo, 1)
                dve.wait_ge(row_ps_ready, n + 1)
                one = 1.0 if row in (SCALE_MSA, SCALE_MLP) else 0.0
                nc.vector.scalar_tensor_tensor(rows[:, row, :], ps[n][0:B, :], one, rows[:, row, :], ALU.add, ALU.add).then_inc(rows_ready, 1)
                if row in (GATE_MSA, GATE_MLP):
                    bias = BIAS_MSA if row == GATE_MSA else BIAS_MLP
                    dve.wait_ge(rows_ready, n + 1)
                    nc.vector.tensor_tensor(rows[:, bias, :], rows[:, bias, :], rows[:, row, :], ALU.mult).then_inc(bias_gated, 1)
                if n == 1:
                    dve.wait_ge(rows_ready, 2)
                    nc.vector.tensor_tensor(rows[:, SLN_S, :], rows[:, GAMMA, :], lngb4[:, 0, :], ALU.mult).then_inc(gb_step, 1)
                    nc.vector.tensor_tensor(rows[:, SLN_T, :], rows[:, GAMMA, :], lngb4[:, 1, :], ALU.mult).then_inc(gb_step, 1)
                    dve.wait_ge(gb_step, 2)
                    nc.vector.tensor_tensor(rows[:, SLN_T, :], rows[:, SLN_T, :], rows[:, BETA, :], ALU.add).then_inc(gb_step, 1)
            dve.wait_ge(turned_ready, 1)
            nc.vector.tensor_copy(sh.mod[:].rearrange("p a k b -> p (a k b)"), ps[0][:, 0:len(TURNED) * KT * B]).then_inc(mod_ready, 1)

        @block.gpsimd
        def _(pool):
            nc.gpsimd.memset(sh.minus_half[:], -0.5)
            nc.gpsimd.memset(sh.eps[:, 0], L0_EPS)
            nc.gpsimd.memset(sh.eps[:, 1], L1_EPS).then_inc(ve_ready, 1)
            pool.wait_ge(mv_ready, TT)
            pool.wait_ge(ve_ready, 1)
            nc.gpsimd.tensor_tensor(ve[:], mv[:, :, 1], sh.eps[:, 0], ALU.add).then_inc(ve_ready, 1)
            pool.wait_ge(ve_ready, 2)
            nc.gpsimd.tensor_tensor(rstd[:], ve[:], sh.minus_half[:], ALU.pow).then_inc(rstd_ready, 1)
            pool.wait_ge(gb_step, 3)
            for row in SPREAD_ORDER:
                if row in ROW_ORDER:
                    pool.wait_ge(rows_ready, ROW_ORDER.index(row) + 1)
                elif row in (BIAS_MSA, BIAS_MLP):
                    pool.wait_ge(bias_gated, 1 if row == BIAS_MSA else 2)
                pool.dma_start(sh.rows_d[SPREAD.index(row)], rows[:, row, :]).then_inc(rows_stored, 16)
            pool.wait_ge(rows_stored, 16 * len(SPREAD))
            pool.wait_ge(mod_ready, 1)
            pool.wait_ge(xn_ready, TT)
            pool.wait_ge(w_lo, 2)


def l0_stage(nc, sh, x_in, weights, wqkv):
    with ExitStack() as ctx:
        def sb(name, shape, dt=F32):
            return ctx.enter_context(nc.sbuf_tensor(name, shape, dt))

        def sem(name):
            return ctx.enter_context(nc.semaphore(name))

        x = sh.xa
        x1 = sb("l0_x1", [P, 2, TT, D])
        nt = sh.nt
        xn = [sh.xn1, sh.xn2]
        ht = sb("l0_ht", [P, 2, KT, CH], F32R)
        hf = sb("l0_hf", [P, 2, FT, CH], F32R)
        gt = sb("l0_gt", [P, 2, CH])
        gate = sb("l0_gate", [P, 2, D])
        gated_bias = sb("l0_gated_bias", [P, 2, D])
        stats = sb("l0_stats", [P, 2, TT, 6])
        mv = sb("l0_mv", [P, 2, TT, 2])
        ve = sb("l0_ve", [P, 2, TT])
        rstd = sb("l0_rstd", [P, 2, TT])

        x_loaded = sem("l0_x_loaded")
        gate_loaded = [sem("l0_gate_msa_loaded"), sem("l0_gate_mlp_loaded")]
        bias_loaded = [sem("l0_bias_msa_loaded"), sem("l0_bias_mlp_loaded")]
        biased = [sem("l0_x_biased"), sem("l0_x1_biased")]
        xn_ready = [sem("l0_xn1_ready"), sem("l0_xn2_ready")]
        turned = [sem("l0_t1_done"), sem("l0_t2_done")]
        turned_taken = [sem("l0_t1_taken"), sem("l0_t2_taken")]
        gt_full = sem("l0_gt_full")
        gt_hi = sem("l0_gt_hi")
        gt_lo = sem("l0_gt_lo")
        l1_done = sem("l0_l1_done")
        l2_done = sem("l0_l2_done")
        f1_done = sem("l0_f1_done")
        f2_done = sem("l0_f2_done")
        gated = [sem("l0_l2_gated"), sem("l0_f2_gated")]
        x1_ready = sem("l0_x1_ready")
        x2_ready = sem("l0_x2_ready")
        x1_free = sem("l0_x1_free")
        ff_loaded = [sem(f"l0_ff{n}_loaded") for n in range(4)]
        ff_hi, ff1_lo, ff2_lo = sem("l0_ff_hi"), sem("l0_ff1_lo"), sem("l0_ff2_lo")
        first_x2_loaded = sem("l0_first_x2_loaded")
        qkv_loaded = [sem(f"l0_qkv{c}_loaded") for c in range(3)]
        qkv_hi = sem("l0_qkv_hi")
        stats_ready = [sem("l0_stats1_ready"), sem("l0_stats2_ready")]
        mv_ready = [sem("l0_mv1_ready"), sem("l0_mv2_ready")]
        ve_ready = [sem("l0_ve1_ready"), sem("l0_ve2_ready")]
        rstd_ready = [sem("l0_rstd1_ready"), sem("l0_rstd2_ready")]

        ps = sh.ps
        w1 = [sh.w0[:, a, 0, :].rearrange("p (k n) -> p k n", k=KT) for a in (HI, LO)]
        w2 = [sh.w0[:, a, 1, :].rearrange("p (k n) -> p k n", k=KT) for a in (HI, LO)]
        fw1 = [sh.w0[:, a, 2:4, :].rearrange("p a (k n) -> p (a k) n", n=FF) for a in (HI, LO)]
        fw2 = [sh.w0[:, a, 4:6, :].rearrange("p a (k n) -> p (a k) n", n=D) for a in (HI, LO)]
        x_v = x_in.rearrange("(s t p) d -> s p t d", s=NCH, p=P)
        x2_v = sh.x2_d.rearrange("(s t p) d -> s p t d", s=NCH, p=P)

        PER = 4 + KT + KT + FT
        U_L1, U_T2, U_T1, U_F1 = 0, 4, 8, 12

        def uses(s, at):
            return at - U_T1 if s is None else KT + PER * s + at

        def before(s):
            return None if isinstance(s, int) and s == 0 else s - 1

        def banks(parity, flip):
            lo = 4 * ((parity + flip) % 2)
            return ps[lo:lo + 4]

        block = ctx.enter_context(nc.Block())

        @block.sync
        def _(sp):
            def load_x(s):
                sp.dma_start(x[:], x_v[s]).then_inc(x_loaded, 16)

            def load_gate(which, b):
                sp.dma_start(gate[:, which, :], sh.rows_d[1 - which, b].partition_broadcast(P)).then_inc(gate_loaded[which], 16)
                sp.dma_start(gated_bias[:, which, :], sh.rows_d[SPREAD.index((BIAS_MSA, BIAS_MLP)[which]), b].partition_broadcast(P)).then_inc(bias_loaded[which], 16)

            def step(s, parity, b_next, first, last):
                if not last:
                    sp.wait_ge(x1_ready, TT * (s + 1))
                    load_x(s + 1)
                    if parity == 1:
                        load_gate(0, b_next)
                if not first:
                    store(s - 1, 1 - parity)
                    if parity == 0 and not last:
                        load_gate(1, b_next)

            def store(s, slot):
                if isinstance(s, int) and s == NCH - 1:
                    for t in range(TT):
                        sp.wait_ge(x2_ready, TT * s + t + 1)
                        sp.dma_start(x2_v[s][:, t], x1[:, slot, t]).then_inc(x1_free, 16)
                    return
                sp.wait_ge(x2_ready, TT * (s + 1))
                sp.dma_start(x2_v[s], x1[:, slot]).then_inc(x1_free, 16)

            def load_qkv(c):
                dst = sh.w0_raw[:, LO, c, :].rearrange("p (k n) -> p k n", k=KT)
                sp.dma_start(dst, wqkv[c].rearrange("(k p) n -> p k n", p=P)).then_inc(qkv_loaded[c], 16)

            load_gate(0, 0)
            load_gate(1, 0)
            for n in range(2, 6):
                sp.dma_start(raw_weight(sh, weights, n), weights[n]).then_inc(ff_loaded[n - 2], 16)
            step(0, 0, None, True, False)
            with sp.Fori(0, 3) as k:
                step(2 * k + 1, 1, k + 1, False, False)
                step(2 * k + 2, 0, k + 1, False, False)
            step(NCH - 1, 1, None, False, True)
            sp.wait_ge(x1_ready, TT * NCH)
            sp.wait_ge(x1_free, 16 * NCH)
            sp.dma_start(x[:], x2_v[0]).then_inc(first_x2_loaded, 16)
            load_qkv(0)
            load_qkv(1)
            sp.wait_ge(f1_done, FT * NCH)
            load_qkv(2)
            store(NCH - 1, 1)
            sp.wait_ge(first_x2_loaded, 16)
            sp.wait_ge(x1_free, 16 * (NCH - 1 + TT + 2))

        @block.tensor
        def _(pe):
            def turn(which, s, half):
                for t in range(TT):
                    if which == 1:
                        pe.wait_ge(xn_ready[which], TT * s + t + 1)
                    elif not (isinstance(s, int) and s == 0):
                        pe.wait_ge(xn_ready[which], TT * (s - 1) + t + 1)
                    for k in range(KT):
                        last = pe.transpose(half[k][:, t * P:(t + 1) * P], xn[which][:, t, k * P:(k + 1) * P], sh.ident[:])
                    last.then_inc(turned[which], 1)

            def to_features(w, src, n_in, ms, half, done):
                for n, m in enumerate(ms):
                    for k in range(n_in):
                        last = split_product(pe, half[n][:], lambda a: w[a][:, k, m * P:(m + 1) * P],
                                             lambda a: src[:, a, k, :], k == 0, k == n_in - 1)
                    last.then_inc(done, 1)

            def to_tokens(w, src, n_in, half, ready_from, done, between=None):
                def add(t, k):
                    return split_product(pe, half[t][:], lambda a: src[:, a, k, t * P:(t + 1) * P],
                                         lambda a: w[a][:, k, :], k == 0, k == n_in - 1)

                for k in range(n_in):
                    if between is not None and k == n_in // 2:
                        between()
                    pe.wait_ge(gt_hi, ready_from + k + 1)
                    pe.wait_ge(gt_lo, ready_from + k + 1)
                    if k < n_in - 2:
                        for t in range(TT):
                            add(t, k)
                for t in range(TT):
                    add(t, n_in - 2)
                    add(t, n_in - 1).then_inc(done, 1)

            def second_ff(s, half, at=U_F1, between=None):
                pe.wait_ge(gt_full, uses(s, at) + TT)
                to_tokens(fw2, hf, FT, half, uses(s, at), f2_done, between)

            def step(s, parity, first, last):
                a, b = banks(parity, 0), banks(parity, 1)
                pe.wait_ge(gt_hi, uses(before(s), U_T1) + KT)
                pe.wait_ge(gt_lo, uses(before(s), U_T1) + KT)
                for m in range(KT):
                    if not first:
                        pe.wait_ge(gt_full, uses(before(s), U_F1) + m + 1)
                    to_features(w1, nt, KT, [m], [a[m]], l1_done)
                to_tokens(w2, ht, KT, b, uses(s, U_L1), l2_done)

                def turn_ln2():
                    pe.wait_ge(x1_ready, TT * (s + 1))
                    turn(1, s, b)

                if first:
                    turn_ln2()
                else:
                    second_ff(before(s), a, between=turn_ln2)
                if first:
                    pe.wait_ge(ff1_lo, 2)
                pe.wait_ge(gt_full, uses(s, U_T2) + KT)
                for k in range(KT):
                    if k == KT // 2 and not last:
                        if not first:
                            pe.wait_ge(x2_ready, TT * s)
                        turn(0, s + 1, a)
                    pe.wait_ge(gt_hi, uses(s, U_T2) + k + 1)
                    pe.wait_ge(gt_lo, uses(s, U_T2) + k + 1)
                    for m in range(4):
                        ins = split_product(pe, b[m][:], lambda h: fw1[h][:, k, m * P:(m + 1) * P],
                                            lambda h: ht[:, h, k, :], k == 0, k == KT - 1)
                        if k == KT - 1:
                            ins.then_inc(f1_done, 1)
                if last:
                    pe.wait_ge(x2_ready, TT * s)
                for m in range(4):
                    if not last:
                        pe.wait_ge(gt_full, uses(s, U_T1) + m + 1)
                    to_features(fw1, ht, KT, [4 + m], [a[m]], f1_done)

            turn(0, 0, banks(0, 1))
            step(0, 0, True, False)
            pe.wait_ge(ff2_lo, 2)
            with pe.Fori(0, 3) as k:
                step(2 * k + 1, 1, False, False)
                step(2 * k + 2, 0, False, False)
            step(NCH - 1, 1, False, True)
            second_ff(NCH - 1, banks(0, 0), U_F1 - KT)

        @block.scalar
        def _(act):
            def slot_free(u):
                return [] if isinstance(u, int) and u < 2 else [(gt_hi, u - 1), (gt_lo, u - 1)]

            def affine(which, s, prev, b, half):
                for k in range(KT):
                    wait_apart(act, sh.act_passed, [(turned[which], TT * (s + 1))] + slot_free(uses(*prev) + k))
                    nc.scalar.activation(gt[:, k % 2, :], half[k][:], ACT.Identity,
                                         bias=sh.mod[:, 2 * which + 1, k, bass.ds(b, 1)],
                                         scale=sh.mod[:, 2 * which, k, bass.ds(b, 1)]).then_inc(gt_full, 1)

            def gelu(func, done, s, at, ms, col, halves):
                for n, m in enumerate(ms):
                    act.wait_ge(done, len(ms) * s + n + 1)
                    for semaphore, value in slot_free(uses(s, at) + n):
                        act.wait_ge(semaphore, value)
                    nc.scalar.activation(gt[:, n % 2, :], halves[n][:], func,
                                         bias=sh.cols[:, col + m:col + m + 1]).then_inc(gt_full, 1)

            def step(s, parity, b, b_next, last):
                lo, hi = banks(parity, 0), banks(parity, 1)
                gelu(ACT.Gelu, l1_done, s, U_L1, range(KT), C_B1, lo)
                if isinstance(s, int) and s == 0:
                    for n in range(2, 6):
                        act.wait_ge(ff_loaded[n - 2], 16)
                        nc.scalar.copy(sh.w0[:, HI, n, :], sh.w0_raw[:, LO, n, :]).then_inc(ff_hi, 1)
                affine(1, s, (s, U_T2), b, hi)
                if not last:
                    affine(0, s + 1, (s, U_T1), b_next, lo)
                gelu(ACT.Gelu_apprx_tanh, f1_done, s, U_F1 - (KT if last else 0), range(FT), C_FB1, hi + lo)

            affine(0, 0, (None, U_T1), 0, banks(0, 1))
            step(0, 0, 0, 0, False)
            with act.Fori(0, 3) as k:
                step(2 * k + 1, 1, k, k + 1, False)
                step(2 * k + 2, 0, k + 1, k + 1, False)
            step(NCH - 1, 1, B - 1, None, True)
            act.wait_ge(f1_done, FT * NCH)
            for c in range(3):
                act.wait_ge(qkv_loaded[c], 16)
                nc.scalar.copy(sh.w0[:, HI, c, :], sh.w0_raw[:, LO, c, :]).then_inc(qkv_hi, 1)

        @block.vector
        def _(dve):
            def hi_parts(u0, n, dst):
                for i in range(n):
                    dve.wait_ge(gt_full, u0 + i + 1)
                    nc.vector.tensor_copy(dst[:, HI, i, :], gt[:, i % 2, :]).then_inc(gt_hi, 1)

            def ln_stats(which, s, src):
                s = s - (1 - which)
                for t in range(TT):
                    nc.vector.bn_stats(stats[:, which, t, :], src[:, t, :]).then_inc(stats_ready[which], 1)
                for t in range(TT):
                    wait_apart(dve, sh.dve_passed, [(stats_ready[which], TT * s + t + 1)])
                    nc.vector.bn_aggr(mv[:, which, t, :], stats[:, which, t, :]).then_inc(mv_ready[which], 1)

            def ln_apply(which, s, src, dst=None):
                dst = xn[which] if dst is None else dst
                dve.wait_ge(rstd_ready[which], s + which)
                for t in range(TT):
                    if which == 1 and not (isinstance(s, int) and s == 0):
                        dve.wait_ge(turned[which], TT * (s - 1) + t + 1)
                    nc.vector.tensor_scalar(dst[:, t, :], src[:, t, :], mv[:, which, t, 0:1], rstd[:, which, t:t + 1],
                                            ALU.subtract, ALU.mult).then_inc(xn_ready[which], 1)

            def residual(which, s, half, src, dst, done, ready):
                for t in range(TT):
                    dve.wait_ge(done, TT * s + t + 1)
                    dve.wait_ge(biased[which], TT * s + t + 1)
                    nc.vector.tensor_tensor(half[t][:], half[t][:], gate[:, which, :], ALU.mult).then_inc(gated[which], 1)
                    dve.wait_ge(gated[which], TT * s + t + 1)
                    nc.vector.tensor_tensor(dst[:, t, :], half[t][:], src[:, t, :], ALU.add).then_inc(ready, 1)

            def second_residual(s, parity, half, b):
                dve.wait_ge(gate_loaded[1], 16 * (b + 1))
                residual(1, s, half, x1[:, parity], x1[:, parity], f2_done, x2_ready)

            def step(s, parity, b, b_prev, first, last):
                lo, hi = banks(parity, 0), banks(parity, 1)
                hi_parts(uses(s, U_L1), KT, ht)
                if first:
                    for n in range(2, 4):
                        dve.wait_ge(ff_hi, n - 1)
                        split_in_place(nc.vector, sh, n).then_inc(ff1_lo, 1)
                dve.wait_ge(gate_loaded[0], 16 * (b + 1))
                dve.wait_ge(x1_free, 16 * (s + 1))
                residual(0, s, hi, x, x1[:, parity], l2_done, x1_ready)
                dve.wait_ge(x1_ready, TT * (s + 1))
                ln_stats(1, s, x1[:, parity])
                ln_apply(1, s, x1[:, parity])
                if not last:
                    dve.wait_ge(x_loaded, 16 * (s + 1))
                    ln_stats(0, s + 1, x)
                hi_parts(uses(s, U_T2), KT, ht)
                if not last:
                    dve.wait_ge(l1_done, KT * (s + 1))
                    ln_apply(0, s + 1, x)
                if not first:
                    second_residual(s - 1, 1 - parity, lo, b_prev)
                if not last:
                    hi_parts(uses(s, U_T1), KT, nt)
                hi_parts(uses(s, U_F1 - (KT if last else 0)), FT, hf)

            nc.vector.memset(ve[:], 0.0).then_inc(x1_free, 32)
            hi_parts(uses(None, U_T1), KT, nt)
            step(0, 0, 0, None, True, False)
            with dve.Fori(0, 3) as k:
                step(2 * k + 1, 1, k, k, False, False)
                step(2 * k + 2, 0, k + 1, k, False, False)
            step(NCH - 1, 1, B - 1, B - 1, False, True)
            for c in range(3):
                dve.wait_ge(qkv_hi, c + 1)
                split_in_place(nc.vector, sh, c)
            dve.wait_ge(first_x2_loaded, 16)
            ln_stats(0, NCH, x)
            ln_apply(0, NCH, x, xn[1])
            second_residual(NCH - 1, 1, banks(0, 0), B - 1)

        @block.gpsimd
        def _(pool):
            def lo_parts(u0, n, dst):
                for i in range(n):
                    pool.wait_ge(gt_hi, u0 + i + 1)
                    nc.gpsimd.tensor_tensor(dst[:, LO, i, :], gt[:, i % 2, :], dst[:, HI, i, :].bitcast(F32),
                                            ALU.subtract).then_inc(gt_lo, 1)

            def inv_std(which, s, eps=0):
                s = s - (1 - which)
                pool.wait_ge(mv_ready[which], TT * (s + 1))
                nc.gpsimd.tensor_tensor(ve[:, which, :], mv[:, which, :, 1], sh.eps[:, eps], ALU.add).then_inc(ve_ready[which], 1)
                pool.wait_ge(ve_ready[which], s + 1)
                nc.gpsimd.tensor_tensor(rstd[:, which, :], ve[:, which, :], sh.minus_half[:], ALU.pow).then_inc(rstd_ready[which], 1)

            def add_gated_bias(which, s, b, tokens):
                pool.wait_ge(bias_loaded[which], 16 * (b + 1))
                if which == 1:
                    pool.wait_ge(xn_ready[1], TT * (s + 1))
                elif not (isinstance(s, int) and s == 0):
                    pool.wait_ge(xn_ready[0], TT * s)
                for t in range(TT):
                    nc.gpsimd.tensor_tensor(tokens[:, t, :], tokens[:, t, :], gated_bias[:, which, :], ALU.add).then_inc(biased[which], 1)

            def split_ff2(n):
                pool.wait_ge(ff_hi, n - 1)
                split_in_place(nc.gpsimd, sh, n).then_inc(ff2_lo, 1)

            def step(s, parity, b, b_prev, last):
                first = isinstance(s, int) and s == 0
                lo_parts(uses(s, U_L1), KT, ht)
                add_gated_bias(0, s, b, x)
                if first:
                    split_ff2(4)
                else:
                    add_gated_bias(1, s - 1, b_prev, x1[:, 1 - parity])
                inv_std(1, s)
                if not last:
                    inv_std(0, s + 1)
                lo_parts(uses(s, U_T2), KT, ht)
                if not last:
                    lo_parts(uses(s, U_T1), KT, nt)
                if first:
                    split_ff2(5)
                lo_parts(uses(s, U_F1 - (KT if last else 0)), FT, hf)

            lo_parts(uses(None, U_T1), KT, nt)
            step(0, 0, 0, None, False)
            with pool.Fori(0, 3) as k:
                step(2 * k + 1, 1, k, k, False)
                step(2 * k + 2, 0, k + 1, k, False)
            step(NCH - 1, 1, B - 1, B - 1, True)
            add_gated_bias(1, NCH - 1, B - 1, x1[:, 1])
            inv_std(0, NCH, eps=1)


def qkv_stage(nc, sh):
    with ExitStack() as ctx:
        def sb(name, shape, dt=F32):
            return ctx.enter_context(nc.sbuf_tensor(name, shape, dt))

        def sem(name):
            return ctx.enter_context(nc.semaphore(name))

        NM = 2 * KT
        w = sh.w0[:, :, 0:3].rearrange("p a c (k n) -> p a c k n", k=KT)
        x = [sh.xa, sb("qk_x", [P, TT, D])]
        xn = sh.xn2
        nt = sb("qk_nt", [P, 2, 2, KT, CH], F32R)
        gt = sb("qk_gt", [P, KT, CH])
        qk = sb("qk_out", [P, NM, 2, CH], F32R)
        v = sb("qk_v", [P, TT, D])
        bv = sb("qk_bv", [P, D])
        stats = sb("qk_stats", [P, TT, 6])
        mv = sb("qk_mv", [P, TT, 2])
        ve = sb("qk_ve", [P, TT])
        rstd = sb("qk_rstd", [P, TT])

        x_loaded = [sem("qk_x_loaded0"), sem("qk_x_loaded1")]
        stats_ready, mv_ready = sem("qk_stats_ready"), sem("qk_mv_ready")
        ve_ready, rstd_ready = sem("qk_ve_ready"), sem("qk_rstd_ready")
        xn_ready = sem("qk_xn_ready")
        turned = sem("qk_turned")
        gt_full, gt_hi, gt_lo = sem("qk_gt_full"), sem("qk_gt_hi"), sem("qk_gt_lo")
        qk_done = sem("qk_qk_done")
        qk_hi, qk_lo = sem("qk_qk_hi"), sem("qk_qk_lo")
        qk_free = sem("qk_qk_free")
        bv_loaded = sem("qk_bv_loaded")
        v_done, v_ready = sem("qk_v_done"), sem("qk_v_ready")
        v_free = sem("qk_v_free")

        ps = sh.ps
        x_v = sh.x2_d.rearrange("(s t p) d -> s p t d", s=NCH, p=P)
        block = ctx.enter_context(nc.Block())

        @block.sync
        def _(sp):
            def load_x(s, slot):
                sp.dma_start(x[slot][:], x_v[s]).then_inc(x_loaded[slot], 16)

            def step(b, half):
                s = 2 * b + half
                for m in range(NM):
                    sp.wait_ge(qk_lo, NM * s + m + 1)
                    dst = sh.qk_d[m // KT, :, KT * b + m % KT, :, half * CH:(half + 1) * CH]
                    sp.dma_start(dst.rearrange("h p n -> p h n"), qk[:, m].bitcast(F32)).then_inc(qk_free, 16)

            load_x(1, 1)
            with sp.Fori(0, B - 1) as b:
                for half in range(2):
                    sp.wait_ge(xn_ready, TT * (2 * b + half + 1))
                    load_x(2 * b + half + 2, half)
                    step(b, half)
            sp.wait_ge(qk_free, 16 * NM * 3)
            load_stack(sp, sh, sh.early_qs, sh.early_ks, 0, RING - 1)
            step(B - 1, 0)
            step(B - 1, 1)
            sp.wait_ge(qk_free, 16 * NM * (NCH + 1))
            sp.wait_ge(sh.stack_loaded[RING - 1], 16 * STACK_LOADS)

        @block.tensor
        def _(pe):
            def turn(s, lo=0):
                if lo is not None:
                    pe.wait_ge(qk_lo, lo)
                for t in range(TT):
                    pe.wait_ge(xn_ready, TT * s + t + 1)
                    for k in range(KT):
                        last = pe.transpose(ps[k][:, t * P:(t + 1) * P], xn[:, t, k * P:(k + 1) * P], sh.ident[:])
                    last.then_inc(turned, 1)

            def step(s, parity, last):
                first = isinstance(s, int) and s == 0
                if first:
                    pe.wait_ge(gt_full, KT)
                for k in range(KT if first else 0):
                    pe.wait_ge(gt_hi, k + 1)
                    pe.wait_ge(gt_lo, k + 1)
                    for m in range(KT):
                        ins = split_product(pe, ps[m][:], lambda a: w[:, a, 0, k, m * P:(m + 1) * P],
                                            lambda a: nt[:, parity, a, k, :], k == 0, k == KT - 1)
                        if k == KT - 1:
                            ins.then_inc(qk_done, 1)
                pe.wait_ge(gt_hi, KT * (s + 1))
                pe.wait_ge(gt_lo, KT * (s + 1))
                for m in range(KT if first else 0, NM):
                    if m >= KT and not (isinstance(s, int) and s == 0):
                        pe.wait_ge(v_ready, TT * (s - 1) + m - KT + 1)
                    for k in range(KT):
                        ins = split_product(pe, ps[m][:], lambda a: w[:, a, m // KT, k, (m % KT) * P:(m % KT + 1) * P],
                                            lambda a: nt[:, parity, a, k, :], k == 0, k == KT - 1)
                    ins.then_inc(qk_done, 1)
                if not last:
                    turn(s + 1, NM * s + KT)
                for t in range(TT):
                    pe.wait_ge(qk_lo, NM * s + KT + t + 1)
                    out = ps[KT + t]
                    for k in range(KT):
                        ins = split_product(pe, out[:], lambda a: nt[:, parity, a, k, t * P:(t + 1) * P],
                                            lambda a: w[:, a, 2, k, :], k == 0, k == KT - 1)
                    ins.then_inc(v_done, 1)

            turn(0, None)
            step(0, 0, False)
            with pe.Fori(0, B - 1) as b:
                step(2 * b + 1, 1, False)
                step(2 * b + 2, 0, False)
            step(NCH - 1, 1, True)

        @block.scalar
        def _(act):
            def styled(s, b):
                for k in range(KT):
                    waits = [(turned, TT * (s + 1))]
                    if not (isinstance(s, int) and s == 0):
                        waits += [(gt_hi, KT * (s - 1) + k + 1), (gt_lo, KT * (s - 1) + k + 1)]
                    wait_apart(act, sh.act_passed, waits)
                    nc.scalar.activation(gt[:, k, :], ps[k][:], ACT.Identity,
                                         bias=sh.mod[:, 5, k, bass.ds(b, 1)],
                                         scale=sh.mod[:, 4, k, bass.ds(b, 1)]).then_inc(gt_full, 1)

            def step(s, b, b_next, half):
                for m in range(NM):
                    act.wait_ge(qk_done, NM * s + m + 1)
                    act.wait_ge(qk_free, 16 * NM * (s + 1))
                    nc.scalar.activation(qk[:, m, HI, :], ps[m][:], ACT.Identity,
                                         bias=sh.cols[:, C_BQ + m:C_BQ + m + 1]).then_inc(qk_hi, 1)
                if b_next is not None:
                    styled(s + 1, b_next)
                def store(t):
                    act.wait_ge(v_ready, TT * s + t + 1)
                    dst = sh.v_d[bass.ds(KT * b, KT), :, half * TT + t, :]
                    act.dma_start(dst.rearrange("g p f -> p g f"),
                                  v[:, t, :].rearrange("p (g f) -> p g f", g=KT)).then_inc(v_free, 16)

                for t in range(TT):
                    store(t)

            act.dma_start(bv[:], sh.biasrows_in[R_BV].partition_broadcast(P)).then_inc(bv_loaded, 16)
            styled(0, 0)
            step(0, 0, 0, 0)
            with act.Fori(0, B - 1) as b:
                step(2 * b + 1, b, b + 1, 1)
                step(2 * b + 2, b + 1, b + 1, 0)
            step(NCH - 1, B - 1, None, 1)
            act.wait_ge(v_free, 16 * TT * (NCH + 1))

        @block.vector
        def _(dve):
            def norm(s, slot, loads):
                dve.wait_ge(x_loaded[slot], 16 * loads)
                for t in range(TT):
                    nc.vector.bn_stats(stats[:, t, :], x[slot][:, t, :]).then_inc(stats_ready, 1)
                for t in range(TT):
                    wait_apart(dve, sh.dve_passed, [(stats_ready, TT * (s - 1) + t + 1)])
                    nc.vector.bn_aggr(mv[:, t, :], stats[:, t, :]).then_inc(mv_ready, 1)
                dve.wait_ge(rstd_ready, s)
                for t in range(TT):
                    dve.wait_ge(turned, TT * (s - 1) + t + 1)
                    nc.vector.tensor_scalar(xn[:, t, :], x[slot][:, t, :], mv[:, t, 0:1], rstd[:, t:t + 1],
                                            ALU.subtract, ALU.mult).then_inc(xn_ready, 1)

            def hi_parts(s, parity):
                for k in range(KT):
                    dve.wait_ge(gt_full, KT * s + k + 1)
                    nc.vector.tensor_copy(nt[:, parity, HI, k, :], gt[:, k, :]).then_inc(gt_hi, 1)

            def step(s, parity, loads):
                if loads is not None:
                    norm(s + 1, 1 - parity, loads)
                for m in range(NM):
                    dve.wait_ge(qk_hi, NM * s + m + 1)
                    nc.vector.scalar_tensor_tensor(qk[:, m, LO, :], ps[m][:], sh.cols[:, C_BQ + m:C_BQ + m + 1],
                                                   qk[:, m, HI, :].bitcast(F32), ALU.add, ALU.subtract).then_inc(qk_lo, 1)
                if loads is not None:
                    hi_parts(s + 1, 1 - parity)
                if isinstance(s, int) and s == 0:
                    dve.wait_ge(bv_loaded, 16)
                dve.wait_ge(v_free, 16 * TT * (s + 1))
                for t in range(TT):
                    dve.wait_ge(v_done, TT * s + t + 1)
                    nc.vector.tensor_tensor(v[:, t, :], ps[KT + t][:], bv[:], ALU.add).then_inc(v_ready, 1)

            nc.vector.memset(ve[:], 0.0).then_inc(qk_free, 16 * NM)
            nc.vector.memset(rstd[:], 0.0).then_inc(v_free, 16 * TT)
            nc.vector.memset(mv[:], 0.0).then_inc(x_loaded[0], 16)
            nc.vector.memset(stats[:], 0.0).then_inc(xn_ready, TT)
            dve.wait_ge(x_loaded[0], 16)
            dve.wait_ge(xn_ready, TT)
            hi_parts(0, 0)
            step(0, 0, 1)
            nc.vector.memset(sh.early_ks[96:98, RING - 1].bitcast(F32), 1.0)
            with dve.Fori(0, B - 1) as b:
                step(2 * b + 1, 1, b + 2)
                step(2 * b + 2, 0, b + 2)
            step(NCH - 1, 1, None)

        @block.gpsimd
        def _(pool):
            def inv_std(s):
                pool.wait_ge(mv_ready, TT * s)
                nc.gpsimd.tensor_tensor(ve[:], mv[:, :, 1], sh.eps[:, 1], ALU.add).then_inc(ve_ready, 1)
                pool.wait_ge(ve_ready, s)
                nc.gpsimd.tensor_tensor(rstd[:], ve[:], sh.minus_half[:], ALU.pow).then_inc(rstd_ready, 1)

            def lo_parts(s, parity):
                for k in range(KT):
                    pool.wait_ge(gt_hi, KT * s + k + 1)
                    nc.gpsimd.tensor_tensor(nt[:, parity, LO, k, :], gt[:, k, :],
                                            nt[:, parity, HI, k, :].bitcast(F32), ALU.subtract).then_inc(gt_lo, 1)

            lo_parts(0, 0)
            inv_std(1)
            lo_parts(1, 1)
            with pool.Fori(1, B) as b:
                inv_std(2 * b)
                lo_parts(2 * b, 0)
                inv_std(2 * b + 1)
                lo_parts(2 * b + 1, 1)


def attention_stage(nc, sh, wp_t):
    with ExitStack() as ctx:
        def sb(name, shape, dt=F32):
            return ctx.enter_context(nc.sbuf_tensor(name, shape, dt))

        def sem(name):
            return ctx.enter_context(nc.semaphore(name))

        STEPS = QH * KC
        PAIRS = STEPS // 2
        UNITS = HG * TT
        LEAD = 13
        SWITCH = STEPS - LEAD
        TURN = (SWITCH + KC, SWITCH)
        PIECES = KC
        PC = CH // PIECES
        sh.projection_tiles = [t for t in early(nc, *PROJECTION_TILES) if "gap" not in t.name]
        sb("at_stacks_place", [P, 2 * RING * HG * N])
        qs, ks = sh.early_qs, sh.early_ks
        a_f, _, a_s, _ = sh.projection_tiles
        v = sb("at_v", [P, RING, KC, P])
        probs = sb("at_probs", [P, 4, HG, CH])
        psum2 = sb("at_pair", [P, 2, HG, CH])
        av_sb = sb("at_av_sb", [P, QH, CH])
        den_sb = sb("at_den_sb", [P, QH, CH])
        rden = sb("at_rden", [P, QH, CH])
        out = sb("at_out", [P, QH, CH])
        mrow = sb("at_mrow", [P, QH, UNITS])
        neg = sb("at_neg", [P, 2, UNITS])
        neg_t = sb("at_neg_t", [2 * UNITS, P])
        ones_col = sb("at_ones_col", [P, HD])
        wp_raw = sb("at_wp_raw", [P, KT, D])

        stack_loaded = sh.stack_loaded
        negm_loaded = sem("at_negm_loaded")
        ones_ready, ones_col_ready = sem("at_ones_ready"), sem("at_ones_col_ready")
        et_done, exp_done = sem("at_et_done"), sem("at_exp_done")
        e_done, max_done = sem("at_e_done"), sem("at_max_done")
        neg_ready = sem("at_neg_ready")
        negt_done, negt_taken = sem("at_negt_done"), sem("at_negt_taken")
        av_done, av_taken = sem("at_av_done"), sem("at_av_taken")
        pair_ready = sem("at_pair_ready")
        den_done, den_taken = sem("at_den_done"), sem("at_den_taken")
        rden_ready = sem("at_rden_ready")
        out_ready = sem("at_out_ready")
        wp_loaded, wp_split = sem("at_wp_loaded"), sem("at_wp_split")
        out_free = sh.out_free

        et = sh.ps[0:2]
        e_ps = [sh.psum[:, 2:4], sh.psum[:, 4:6]]
        av_ps, den_ps = sh.ps[6], sh.ps[7]
        SOFTMAX_SCALE = float(D) ** -0.5
        LOADS = 16 * (STACK_LOADS + 1)

        def halves(g, h):
            return QH * g + h + 1

        def groups(eng, group):
            group(0, 2, nth=0, first=True)
            with eng.Fori(0, 4) as k:
                for i in range(RING):
                    group(3 * k + i + 1, i, nth=k + (i + 2) // RING)
            group(13, 0, nth=4)
            group(14, 1, nth=5, load=False)
            group(15, 2, load=False, with_next=False)

        def units_of_step(g, slot, i, with_next):
            if i >= SWITCH and not with_next:
                return []
            whose, at = (g + 1, (slot + 1) % RING) if i >= SWITCH else (g, slot)
            n = 2 * ((i - SWITCH) % STEPS)
            return [(whose, at, (n + a) // UNITS, (n + a) % UNITS, QH * UNITS * whose + n + a) for a in range(2)]

        FIRST_UNITS = 2 * LEAD

        block = ctx.enter_context(nc.Block())

        @block.sync
        def _(sp):
            def load_group(g, slot):
                load_stack(sp, sh, qs, ks, g, slot)
                load_v(g, slot)

            def load_v(g, slot):
                sp.dma_start(v[:, slot], sh.v_d[g]).then_inc(stack_loaded[slot], 16)

            def place_neg(g, slot, half):
                sp.wait_ge(negt_taken, halves(g, half))
                for part in range(2):
                    dst = qs[96 + part:97 + part, slot, half].bitcast(F32).rearrange("o j (c q) -> o (j c) q", q=P)
                    sp.dma_start(dst, neg_t[part * UNITS:(part + 1) * UNITS, :]).then_inc(negm_loaded, 16)

            def store(g, half):
                sp.wait_ge(out_ready, halves(g, half))
                sp.dma_start(sh.at_d[g, :, half * CH:(half + 1) * CH], out[:, half]).then_inc(out_free[half], 16)

            def group(g, slot, nth=None, first=False, load=True, with_next=True):
                if not with_next:
                    sp.wait_ge(av_done, STEPS * g)
                    for half in range(QH):
                        sp.wait_ge(out_free[half], 16 * (KT + 1))
                    x, st = sh.projection_tiles[1], sh.projection_tiles[3]
                    for half in range(QH):
                        load_projection_input(sp, sh, a_f, x, st, 0, half)
                if not first and load:
                    sp.wait_ge(av_done, STEPS * g)
                    load_group(g + 2, (slot + 2) % RING)
                place_neg(g, slot, 1)
                if not first:
                    store(g - 1, 0)
                if with_next:
                    place_neg(g + 1, (slot + 1) % RING, 0)
                if not first:
                    store(g - 1, 1)

            load_v(0, RING - 1)
            load_group(1, 0)
            place_neg(0, RING - 1, 0)
            load_group(2, 1)
            groups(sp, group)
            for half in range(QH):
                store(G - 1, half)
            for half in range(QH):
                sp.wait_ge(sh.a_loaded[half], 16 * KT)
                sp.wait_ge(sh.x_loaded[half], 16)
                sp.wait_ge(sh.st_loaded[half], 32)

        @block.tensor
        def _(pe):
            def max_unit(unit, keys):
                g, slot, half, u, n = unit
                j, c = u // TT, u % TT
                if keys == 0 and not (isinstance(n, int) and n < 2):
                    pe.wait_ge(max_done, n - 1)
                pe.matmul(e_ps[u % 2][:, keys, :], qs[0:96, slot, half, j, c * P:(c + 1) * P],
                          ks[0:96, slot, j, keys * CH:(keys + 1) * CH], start=True, stop=True).then_inc(e_done, 1)

            def turn_neg(g, half):
                pe.wait_ge(neg_ready, 2 * halves(g, half))
                if not (isinstance(g, int) and g == 0):
                    pe.wait_ge(den_taken, halves(g, half) - 2)
                pe.transpose(den_ps[0:2 * UNITS, 0:P], neg[:].rearrange("p a n -> p (a n)"), sh.ident[:]).then_inc(negt_done, 1)

            def energies(g, slot, i, j):
                if not (isinstance(g, int) and HG * (STEPS * g + i) + j < 2):
                    pe.wait_ge(exp_done, HG * (STEPS * g + i) + j - 1)
                pe.matmul(et[j % 2][:], ks[0:98, slot, j, (i % KC) * P:(i % KC + 1) * P],
                          qs[0:98, slot, i // KC, j, :], start=True, stop=True).then_inc(et_done, 1)

            def av(g, slot, i):
                kc = i % KC
                pe.wait_ge(exp_done, HG * (STEPS * g + i + 1))
                if kc == 0 and not (isinstance(g, int) and g == 0 and i == 0):
                    pe.wait_ge(av_taken, QH * g + i // KC)
                for j in range(HG):
                    rows = slice(HD * j, HD * (j + 1))
                    last = pe.matmul(av_ps[rows, :], v[:, slot, kc, rows], probs[:, kc % 4, j, :],
                                     start=kc == 0, stop=kc == KC - 1)
                last.then_inc(av_done, 1)

            def den(g, pair, turned=None):
                pe.wait_ge(pair_ready, PAIRS * g + pair + 1)
                n = pair % (KC // 2)
                if n == 0 and not (isinstance(g, int) and g == 0 and pair == 0):
                    pe.wait_ge(den_taken, QH * g + pair // (KC // 2))
                if turned is not None:
                    pe.wait_ge(negt_taken, turned)
                for j in range(HG):
                    rows = slice(HD * j, HD * (j + 1))
                    last = pe.matmul(den_ps[rows, :], ones_col[:], psum2[:, pair % 2, j, :],
                                     start=n == 0, stop=n == KC // 2 - 1)
                last.then_inc(den_done, 1)

            def group(g, slot, nth=None, first=False, load=True, with_next=True):
                nxt = (slot + 1) % RING
                prev = (slot + 2) % RING
                for i in range(STEPS):
                    if i % KC == 0:
                        pe.wait_ge(negm_loaded, 32 * halves(g, i // KC))
                    if with_next and i == SWITCH:
                        pe.wait_ge(stack_loaded[nxt], LOADS * (nth + 1))
                    products = [(unit, keys) for unit in units_of_step(g, slot, i, with_next) for keys in range(2)]
                    if i % 2 == 1:
                        products += [(unit, 0) for unit in units_of_step(g, slot, i + 1, with_next)[0:1]]
                        behind = (1, 1, 1, 2)
                    elif first and i == 0:
                        behind = (2, 0, 1, 1)
                    else:
                        products = products[1:]
                        behind = (1, 0, 1, 1)
                    for j in range(HG):
                        energies(g, slot, i, j)
                        for product in products[sum(behind[:j]):sum(behind[:j + 1])]:
                            max_unit(*product)
                        if j == 1:
                            if i >= 1:
                                av(g, slot, i - 1)
                            elif not first:
                                av(g - 1, prev, STEPS - 1)
                    if i % 2 == 0:
                        if i >= 4:
                            turned = {4: halves(g, 1), 12: halves(g + 1, 0) if with_next else None}.get(i)
                            den(g, (i - 4) // 2, turned)
                        elif not first:
                            den(g - 1, PAIRS - 2 + i // 2)
                    if i == TURN[1]:
                        turn_neg(g, 1)
                    if with_next and i == TURN[0]:
                        turn_neg(g + 1, 0)

            pe.wait_ge(stack_loaded[RING - 1], 16 * STACK_LOADS)
            for n in range(FIRST_UNITS):
                if n == UNITS + 2:
                    turn_neg(0, 0)
                for keys in range(2):
                    max_unit((0, RING - 1, n // UNITS, n % UNITS, n), keys)
            pe.wait_ge(ones_ready, 1)
            pe.wait_ge(ones_col_ready, 1)
            pe.wait_ge(stack_loaded[RING - 1], LOADS)
            groups(pe, group)
            av(G - 1, RING - 1, STEPS - 1)
            den(G - 1, PAIRS - 2)
            for n in (2, 3):
                for j in range(HG):
                    last = pe.matmul(den_ps[HD * j:HD * (j + 1), :], ones_col[:], probs[:, n, j, :], start=False, stop=n == 3)
            last.then_inc(den_done, 1)

        @block.scalar
        def _(act):
            def take_neg(g, half):
                act.wait_ge(negt_done, halves(g, half))
                if not (isinstance(g, int) and g == 0 and half == 0):
                    act.wait_ge(negm_loaded, 32 * (halves(g, half) - 1))
                nc.scalar.copy(neg_t[:], den_ps[0:2 * UNITS, 0:P]).then_inc(negt_taken, 1)

            def take_av(g, half):
                act.wait_ge(av_done, STEPS * g + KC * (half + 1))
                if not (isinstance(g, int) and g == 0):
                    act.wait_ge(out_ready, halves(g, half) - 2)
                nc.scalar.activation(av_sb[:, half], av_ps[:], ACT.Copy, scale=SOFTMAX_SCALE).then_inc(av_taken, 1)

            def take_den(g, half):
                act.wait_ge(den_done, KC // 2 * halves(g, half))
                if not (isinstance(g, int) and g == 0):
                    act.wait_ge(rden_ready, PIECES * (halves(g, half) - 2))
                nc.scalar.copy(den_sb[:, half], den_ps[:]).then_inc(den_taken, 1)

            def group(g, slot, nth=None, first=False, load=True, with_next=True):
                for i in range(STEPS):
                    if not (first and i < 4):
                        act.wait_ge(av_done, STEPS * g + i - 3)
                        act.wait_ge(pair_ready, PAIRS * g + (i - 4) // 2 + 1)
                    if not with_next and KC // 2 <= i < KC // 2 + 2 * KT:
                        half, k = divmod(i - KC // 2, KT)
                        act.wait_ge(sh.a_loaded[half], 16 * KT)
                        nc.scalar.copy(a_s[:, half, HI, k], a_f[:, half, k]).then_inc(sh.a_hi, 1)
                    for j in range(HG):
                        act.wait_ge(et_done, HG * (STEPS * g + i) + j + 1)
                        nc.scalar.activation(probs[:, i % 4, j, :], et[j % 2][:], ACT.Exp).then_inc(exp_done, 1)
                        if j == 1 and i == KC:
                            take_av(g, 0)
                        if j == 1 and i == 0 and not first:
                            take_av(g - 1, 1)
                    if i == 2 and not first:
                        take_den(g - 1, 1)
                    if i == KC + 2:
                        take_den(g, 0)
                    if i == TURN[1]:
                        take_neg(g, 1)
                    if with_next and i == TURN[0]:
                        take_neg(g + 1, 0)

            act.dma_start(wp_raw[:], wp_t.rearrange("(k p) n -> p k n", p=P)).then_inc(wp_loaded, 16)
            act.wait_ge(wp_loaded, 16)
            nc.scalar.copy(sh.wp[:, HI], wp_raw[:]).then_inc(wp_split, 1)
            take_neg(0, 0)
            groups(act, group)
            take_av(G - 1, 1)
            take_den(G - 1, 1)

        @block.vector
        def _(dve):
            def take_max(g, slot, half, u, n):
                dve.wait_ge(e_done, 2 * (n + 1))
                nc.vector.tensor_reduce(mrow[:, half, u:u + 1], e_ps[u % 2], AX.XY, ALU.max).then_inc(max_done, 1)

            def negate_max(g, half):
                dve.wait_ge(max_done, UNITS * halves(g, half))
                if not (isinstance(g, int) and g == 0 and half == 0):
                    dve.wait_ge(negt_done, halves(g, half) - 1)
                nc.vector.tensor_scalar(neg[:, HI, :].bitcast(F32R), mrow[:, half], -1.0, None, ALU.mult).then_inc(neg_ready, 1)
                dve.wait_ge(neg_ready, 2 * halves(g, half) - 1)
                nc.vector.scalar_tensor_tensor(neg[:, LO, :], mrow[:, half], -1.0, neg[:, HI, :], ALU.mult, ALU.subtract).then_inc(neg_ready, 1)

            def invert(g, half, piece):
                if piece == 0:
                    dve.wait_ge(den_taken, halves(g, half))
                    if not (isinstance(g, int) and g == 0):
                        dve.wait_ge(out_ready, halves(g, half) - 2)
                cols = slice(piece * PC, (piece + 1) * PC)
                nc.vector.reciprocal(rden[:, half, cols], den_sb[:, half, cols]).then_inc(rden_ready, 1)

            def group(g, slot, nth=None, first=False, load=True, with_next=True):
                for i in range(STEPS):
                    units = units_of_step(g, slot, i, with_next)
                    for unit in units[0:1]:
                        take_max(*unit)
                    if i >= 12:
                        for piece in ([i - 12] if with_next else [2 * (i - 12), 2 * (i - 12) + 1]):
                            invert(g, 0, piece)
                    elif not first:
                        invert(g - 1, *((1, i - 4) if i >= 4 else (0, i + 4)))
                    for unit in units[1:2]:
                        take_max(*unit)
                    if not with_next and KC // 2 <= i < KC // 2 + 2 * KT:
                        half, k = divmod(i - KC // 2, KT)
                        dve.wait_ge(sh.a_hi, KT * half + k + 1)
                        nc.vector.tensor_tensor(a_s[:, half, LO, k], a_f[:, half, k], a_s[:, half, HI, k].bitcast(F32),
                                                ALU.subtract).then_inc(sh.a_lo_last if k == KT - 1 else sh.a_lo, 1)
                    if i == TURN[1] - 1:
                        negate_max(g, 1)
                    if with_next and i == TURN[0] - 1:
                        negate_max(g + 1, 0)

            nc.vector.memset(ones_col[:], 1.0).then_inc(ones_col_ready, 1)
            nc.vector.memset(mrow[:], 0.0).then_inc(out_free[0], 16)
            nc.vector.memset(neg[:], 0.0).then_inc(out_free[1], 16)
            dve.wait_ge(out_free[0], 16)
            dve.wait_ge(out_free[1], 16)
            for n in range(FIRST_UNITS):
                take_max(0, RING - 1, n // UNITS, n % UNITS, n)
                if n == UNITS - 1:
                    negate_max(0, 0)
            groups(dve, group)
            for piece in range(PIECES):
                invert(G - 1, 1, piece)
            dve.wait_ge(rden_ready, PIECES * halves(G - 1, 1))
            dve.wait_ge(av_taken, halves(G - 1, 1))
            dve.wait_ge(out_free[1], 16 * G)
            dve.wait_ge(out_ready, halves(G - 1, 0))
            nc.vector.tensor_tensor(out[:, 1], av_sb[:, 1], rden[:, 1], ALU.mult).then_inc(out_ready, 1)

        @block.gpsimd
        def _(pool):
            def finish(g, half):
                pool.wait_ge(av_taken, halves(g, half))
                pool.wait_ge(rden_ready, PIECES * halves(g, half))
                pool.wait_ge(out_free[half], 16 * (g + 1))
                nc.gpsimd.tensor_tensor(out[:, half], av_sb[:, half], rden[:, half], ALU.mult).then_inc(out_ready, 1)

            def group(g, slot, nth=None, first=False, load=True, with_next=True):
                for pair in range(PAIRS if with_next else PAIRS - 1):
                    if pair in (1, 5) and not first:
                        finish(g - 1, pair // 4)
                    pool.wait_ge(exp_done, HG * (STEPS * g + 2 * pair + 2))
                    if not (first and pair < 2):
                        pool.wait_ge(den_done, PAIRS * g + pair - 1)
                    a = 2 * pair % 4
                    nc.gpsimd.tensor_tensor(psum2[:, pair % 2], probs[:, a], probs[:, a + 1], ALU.add).then_inc(pair_ready, 1)

            nc.gpsimd.memset(ks[96:98, 0:RING - 1].bitcast(F32), 1.0).then_inc(ones_ready, 1)
            pool.wait_ge(ones_ready, 1)
            pool.wait_ge(wp_split, 1)
            nc.gpsimd.tensor_tensor(sh.wp[:, LO], wp_raw[:], sh.wp[:, HI].bitcast(F32), ALU.subtract)
            groups(pool, group)
            finish(G - 1, 0)


SLOT = HG * N
PROJECTION_TILES = (("o_a", [P, 2, KT, CH], F32), ("o_x", [P, 2, TT, D], F32), ("o_gap0", [P, SLOT], F32),
                    ("o_as", [P, 2, 2, KT, CH], F32R), ("o_gap1", [P, SLOT], F32), ("o_st", [P, 2, 2, D], F32))
PROJECTION_WORDS = 2 * KT * CH + 2 * TT * D + 2 * SLOT + 2 * 2 * KT * CH + 2 * 2 * D


def out_stage(nc, sh, y_out):
    with ExitStack() as ctx:
        def sb(name, shape, dt=F32):
            return ctx.enter_context(nc.sbuf_tensor(name, shape, dt))

        def sem(name):
            return ctx.enter_context(nc.semaphore(name))

        sb("o_tiles_place", [P, PROJECTION_WORDS])
        a_f, x, a_s, st = sh.projection_tiles
        h1 = sb("o_h1", [P, 2, TT, D])
        z = sb("o_z", [P, 2, TT, D])
        stats = sb("o_stats", [P, TT, 6])
        mv = sb("o_mv", [P, TT, 2])
        ve = sb("o_ve", [P, TT])
        rstd = sb("o_rstd", [P, TT])
        neg_mean = sb("o_neg_mean", [P, TT])
        shift = sb("o_shift", [P, TT])

        a_loaded, x_loaded, st_loaded = sh.a_loaded, sh.x_loaded, sh.st_loaded
        a_hi, a_lo, a_lo_last = sh.a_hi, sh.a_lo, sh.a_lo_last
        p_done = sem("o_p_done")
        h1_ready = sem("o_h1_ready")
        stats_ready, mv_ready = sem("o_stats_ready"), sem("o_mv_ready")
        ve_ready, rstd_ready, shift_ready = sem("o_ve_ready"), sem("o_rstd_ready"), sem("o_shift_ready")
        neg_mean_ready = sem("o_neg_mean_ready")
        z_norm, z_scaled = sem("o_z_norm"), sem("o_z_scaled")
        h1t_ready = sem("o_h1t_ready")
        y_ready = sem("o_y_ready")
        z_free = [sem("o_z_free0"), sem("o_z_free1")]

        ps = sh.ps
        x_v = sh.x2_d.rearrange("(s t p) d -> s p t d", s=NCH, p=P)
        y_v = y_out.rearrange("(s t p) d -> s p t d", s=NCH, p=P)

        def chunks(eng, chunk):
            for half in range(2):
                chunk(half, 0, half, first=True)
            with eng.Fori(1, B - 1) as b:
                for half in range(2):
                    chunk(2 * b + half, b, half)
            for half in range(2):
                chunk(2 * (B - 1) + half, B - 1, half, last=True)

        block = ctx.enter_context(nc.Block())

        @block.sync
        def _(sp):
            def load_a(b, half):
                for k in range(KT):
                    sp.dma_start(a_f[:, half, k], sh.at_d[KT * b + k, :, half * CH:(half + 1) * CH]).then_inc(a_loaded[half], 16)

            def load_x(b, half):
                sp.dma_start(x[:, half], x_v[2 * b + half]).then_inc(x_loaded[half], 16)

            def load_st(b, half):
                for i in range(2):
                    sp.dma_start(st[:, half, i], sh.rows_d[2 + i, b].partition_broadcast(P)).then_inc(st_loaded[half], 16)

            def chunk(s, b, half, first=False, last=False):
                if not last:
                    sp.wait_ge(a_lo, (KT - 1) * (s + 1))
                    sp.wait_ge(a_lo_last, s + 1)
                    load_a(b + 1, half)
                    sp.wait_ge(h1_ready, TT * (s + 1))
                    load_x(b + 1, half)
                if not (isinstance(s, int) and s == 0):
                    store(s - 1, 1 - half)
                    if not (isinstance(s, int) and s == NCH - 1):
                        load_st(b + half, 1 - half)

            def store(s, half):
                sp.wait_ge(y_ready, TT * (s + 1))
                sp.dma_start(y_v[s], z[:, half]).then_inc(z_free[half], 16)

            for half in range(QH):
                sp.wait_ge(sh.out_free[half], 16 * (G + 1))
            chunks(sp, chunk)
            for t in range(TT):
                sp.wait_ge(y_ready, TT * (NCH - 1) + t + 1)
                sp.dma_start(y_v[NCH - 1][:, t], z[:, 1, t]).then_inc(z_free[1], 16)
            sp.wait_ge(z_free[0], 16 * (B + 1))
            sp.wait_ge(z_free[1], 16 * (B + TT))

        @block.tensor
        def _(pe):
            def chunk(s, b, half, first=False, last=False):
                if not first:
                    pe.wait_ge(h1_ready, TT * (s - 1))
                pe.wait_ge(a_hi, KT * (s + 1))
                pe.wait_ge(a_lo, (KT - 1) * (s + 1))
                pe.wait_ge(a_lo_last, s + 1)
                for t in range(TT):
                    acc = ps[4 * half + t]
                    add_bias(pe, sh, acc[:])
                    for k in range(KT):
                        ins = split_product(pe, acc[:], lambda a: a_s[:, half, a, k, t * P:(t + 1) * P],
                                            lambda a: sh.wp[:, a, k, :], False, k == KT - 1)
                    ins.then_inc(p_done, 1)

            chunks(pe, chunk)

        @block.scalar
        def _(act):
            def hi_parts(s, b, half):
                act.wait_ge(a_loaded[half], 16 * KT * (b + 1))
                act.wait_ge(p_done, TT * (s - 1))
                for k in range(KT):
                    nc.scalar.copy(a_s[:, half, HI, k], a_f[:, half, k]).then_inc(a_hi, 1)

            def chunk(s, b, half, first=False, last=False):
                if not last:
                    hi_parts(s + 2, b + 1, half)
                act.wait_ge(shift_ready, s + 1)
                act.wait_ge(z_free[half], 16 * (b + 1))
                for t in range(TT):
                    nc.scalar.activation(z[:, half, t, :], h1[:, half, t, :], ACT.Identity,
                                         bias=shift[:, t:t + 1], scale=rstd[:, t:t + 1]).then_inc(z_norm, 1)

            chunks(act, chunk)

        @block.vector
        def _(dve):
            def scale(s, half, t):
                dve.wait_ge(z_norm, TT * s + t + 1)
                nc.vector.tensor_tensor(z[:, half, t, :], z[:, half, t, :], st[:, half, 0, :], ALU.mult).then_inc(z_scaled, 1)

            def finish(s, half):
                for t in range(TT):
                    dve.wait_ge(z_scaled, TT * s + t + 1)
                    dve.wait_ge(h1t_ready, TT * s + t + 1)
                    nc.vector.tensor_tensor(z[:, half, t, :], z[:, half, t, :], h1[:, half, t, :], ALU.add).then_inc(y_ready, 1)

            def chunk(s, b, half, first=False, last=False):
                dve.wait_ge(x_loaded[half], 16 * (b + 1))
                alone = isinstance(s, int) and s == 0
                if not alone:
                    dve.wait_ge(st_loaded[1 - half], 32 * (b + half))
                if not first:
                    dve.wait_ge(y_ready, TT * (s - 1))
                for t in range(TT):
                    dve.wait_ge(p_done, TT * s + t + 1)
                    nc.vector.tensor_tensor(h1[:, half, t, :], ps[4 * half + t][:], x[:, half, t, :], ALU.add).then_inc(h1_ready, 1)
                    if not alone:
                        scale(s - 1, 1 - half, t)
                    dve.wait_ge(h1_ready, TT * s + t + 1)
                    nc.vector.bn_stats(stats[:, t, :], h1[:, half, t, :]).then_inc(stats_ready, 1)
                for t in range(TT):
                    wait_apart(dve, sh.dve_passed, [(stats_ready, TT * s + t + 1)])
                    nc.vector.bn_aggr(mv[:, t, :], stats[:, t, :]).then_inc(mv_ready, 1)
                dve.wait_ge(mv_ready, TT * (s + 1))
                if not alone:
                    dve.wait_ge(shift_ready, s)
                nc.vector.tensor_scalar(neg_mean[:], mv[:, :, 0], -1.0, None, ALU.mult).then_inc(neg_mean_ready, 1)
                if not last:
                    lo_part(s + 2, half)
                if not alone:
                    finish(s - 1, 1 - half)

            def lo_part(s, half):
                k = KT - 1
                dve.wait_ge(a_hi, KT * (s + 1))
                nc.vector.tensor_tensor(a_s[:, half, LO, k], a_f[:, half, k], a_s[:, half, HI, k].bitcast(F32),
                                        ALU.subtract).then_inc(a_lo_last, 1)

            nc.vector.memset(rstd[:], 0.0).then_inc(z_free[0], 16)
            nc.vector.memset(ve[:], 0.0).then_inc(z_free[1], 16)
            chunks(dve, chunk)
            dve.wait_ge(st_loaded[1], 32 * B)
            for t in range(TT):
                scale(NCH - 1, 1, t)
            finish(NCH - 1, 1)

        @block.gpsimd
        def _(pool):
            def lo_parts(s, half):
                for k in range(KT - 1):
                    pool.wait_ge(a_hi, KT * s + k + 1)
                    nc.gpsimd.tensor_tensor(a_s[:, half, LO, k], a_f[:, half, k], a_s[:, half, HI, k].bitcast(F32),
                                            ALU.subtract).then_inc(a_lo, 1)

            def chunk(s, b, half, first=False, last=False):
                pool.wait_ge(mv_ready, TT * (s + 1))
                if not (isinstance(s, int) and s == 0):
                    pool.wait_ge(z_norm, TT * s)
                nc.gpsimd.tensor_tensor(ve[:], mv[:, :, 1], sh.eps[:, 1], ALU.add).then_inc(ve_ready, 1)
                pool.wait_ge(ve_ready, s + 1)
                nc.gpsimd.tensor_tensor(rstd[:], ve[:], sh.minus_half[:], ALU.pow).then_inc(rstd_ready, 1)
                pool.wait_ge(rstd_ready, s + 1)
                pool.wait_ge(neg_mean_ready, s + 1)
                nc.gpsimd.tensor_tensor(shift[:], neg_mean[:], rstd[:], ALU.mult).then_inc(shift_ready, 1)
                if not last:
                    lo_parts(s + 2, half)
                pool.wait_ge(st_loaded[half], 32 * (b + 1))
                for t in range(TT):
                    pool.wait_ge(z_norm, TT * s + t + 1)
                    nc.gpsimd.tensor_tensor(h1[:, half, t, :], h1[:, half, t, :], st[:, half, 1, :], ALU.add).then_inc(h1t_ready, 1)

            chunks(pool, chunk)


def build(nc, x, cond_t, ada_w, wg_t, wb_t, row_bias, lngb, colpack, biasrows, neg_mask, ident, w1, w2, fw1, fw2, wqkv, wp_t, y,
          stages=5):
    with ExitStack() as ctx:
        sh = Shared()

        def sb(name, shape, dt=F32):
            return ctx.enter_context(nc.sbuf_tensor(name, shape, dt))

        sh.psum = ctx.enter_context(nc.psum_tensor("banks", [P, 8, CH], F32))
        sh.ps = [sh.psum[:, i] for i in range(8)]
        sh.ident = sb("ident_sb", [P, P])
        sh.cols = sb("cols", [P, NCOL])
        sh.mod = sb("mod", [P, len(TURNED), KT, B])
        sh.ones2 = sb("ones2", [2, P], F32R)
        sh.bias_rows = sb("bias_rows", [2, D], F32R)
        sh.minus_half = sb("minus_half", [P, TT])
        sh.eps = sb("eps", [P, 2, TT])
        sh.act_passed, sh.dve_passed, sh.pe_passed = (ctx.enter_context(nc.semaphore(f"{e}_passed")) for e in ("act", "dve", "pe"))
        sh.biasrows_in = biasrows
        sh.rows_d = nc.dram_tensor("rows_scratch", [len(SPREAD), B, D], F32, kind="Internal").ap()
        sh.x2_d = nc.dram_tensor("x2_scratch", [T, D], F32, kind="Internal").ap()
        sh.qk_d = nc.dram_tensor("qk_scratch", [2, 2, G, P, N], F32, kind="Internal").ap()
        sh.v_d = nc.dram_tensor("v_scratch", [G, P, KC, P], F32, kind="Internal").ap()
        sh.at_d = nc.dram_tensor("attn_scratch", [G, P, N], F32, kind="Internal").ap()

        weights = [w1.rearrange("(k p) n -> p k n", p=P), w2.rearrange("(k p) n -> p k n", p=P)]
        weights += [fw1[256 * i:256 * (i + 1)].rearrange("(k p) n -> p k n", p=P) for i in range(2)]
        weights += [fw2[512 * i:512 * (i + 1)].rearrange("(k p) n -> p k n", p=P) for i in range(2)]
        sh.stack_loaded = [ctx.enter_context(nc.semaphore(f"stack_loaded{i}")) for i in range(RING)]
        sh.a_loaded, sh.x_loaded, sh.st_loaded = ([ctx.enter_context(nc.semaphore(f"o_{n}_loaded{i}")) for i in range(2)]
                                                  for n in ("a", "x", "st"))
        sh.out_free = [ctx.enter_context(nc.semaphore(f"at_out_free{i}")) for i in range(QH)]
        sh.a_hi, sh.a_lo, sh.a_lo_last = (ctx.enter_context(nc.semaphore("o_" + n)) for n in ("a_hi", "a_lo", "a_lo_last"))
        sh.early_qs, sh.early_ks = early(nc, ("early_qs", [P, RING, QH, HG, CH], F32R), ("early_ks", [P, RING, HG, N], F32R))
        with ExitStack() as l0:
            with nc.sbuf_tensor("l0_weights_raw", [P, 2, 6, 2048], F32) as raw:
                sh.w0_raw = raw
            sh.w0 = l0.enter_context(nc.sbuf_tensor("l0_weights", [P, 2, 6, 2048], F32R))
            sh.xa = l0.enter_context(nc.sbuf_tensor("chunk_in", [P, TT, D], F32))
            sh.xn2 = l0.enter_context(nc.sbuf_tensor("tokens_normed", [P, TT, D], F32))
            with ExitStack() as first:
                with nc.sbuf_tensor("l0_nt_raw", [P, 2, TT, D], F32) as raw:
                    sh.xn1 = raw[:, LO]
                sh.nt = first.enter_context(nc.sbuf_tensor("l0_nt", [P, 2, KT, CH], F32R))
                setup_stage(nc, sh, x, cond_t, ada_w, wg_t, wb_t, row_bias, lngb, colpack, neg_mask, ident, weights)
                if stages >= 2:
                    l0_stage(nc, sh, x, weights, wqkv)
            if stages >= 3:
                qkv_stage(nc, sh)
        sh.wp = ctx.enter_context(nc.sbuf_tensor("wp", [P, 2, KT, D], F32R, side="right"))
        if stages >= 4:
            attention_stage(nc, sh, wp_t)
        if stages >= 5:
            out_stage(nc, sh, y)


def layout(i):
    import numpy as np

    a = {k: np.asarray(v) for k, v in i.items()}
    f = "L0_cond_", "L1_cond_"
    cols = lambda v: v.reshape(-1, P).T
    by_kind = a[f[1] + "Wqkv"].reshape(D, 3, D)
    b_kind = a[f[1] + "bqkv"].reshape(D, 3)
    out = {
        "x": a["x"].reshape(T, D),
        "cond_t": a["cond_1024"].T.reshape(KT, P, B).transpose(1, 0, 2),
        "ada_w": a[f[0] + "ada_w"],
        "wg_t": a[f[1] + "Wg"].T,
        "wb_t": a[f[1] + "Wb"].T,
        "row_bias": np.concatenate([a[f[0] + "ada_b"].reshape(6, D), a[f[1] + "bg"][None], a[f[1] + "bb"][None]]),
        "lngb": np.stack([a[f[1] + "ln_g"], a[f[1] + "ln_b"]]),
        "colpack": np.concatenate([cols(a[f[0] + "ssm_b1"]), cols(a[f[0] + "ff_b1"]), cols(b_kind[:, 0]), cols(b_kind[:, 1])], 1),
        "biasrows": np.stack([a[f[0] + "ssm_b2"], a[f[0] + "ff_b2"], b_kind[:, 2], a[f[1] + "bp"]]),
        "neg_mask": np.array([[0.0], [-1.0]], np.float32),
        "ident": np.eye(P, dtype=np.float32),
        "w1": a[f[0] + "ssm_w1"],
        "w2": a[f[0] + "ssm_w2"],
        "fw1": a[f[0] + "ff_w1"],
        "fw2": a[f[0] + "ff_w2"],
        "wqkv": by_kind.transpose(1, 2, 0),
        "wp_t": a[f[1] + "Wp"].T,
    }
    return {k: np.ascontiguousarray(v) for k, v in out.items()}


def kernel(**inputs):
    import concourse.bacc as bacc
    from concourse.bass_utils import run_bass_kernel_spmd

    nc = bacc.Bacc("TRN2", target_bir_lowering=False, num_devices=1)
    arrays = layout(inputs)
    args = {k: nc.dram_tensor(k, v.shape, mybir.dt.from_np(v.dtype), kind="ExternalInput").ap() for k, v in arrays.items()}
    y = nc.dram_tensor("y", (T, D), F32, kind="ExternalOutput").ap()
    build(nc, y=y, **args)
    got = run_bass_kernel_spmd(nc, [arrays], core_ids=[0])
    return got.results[0]["y"].reshape(B, N, D)
```
